# Optimizing a Trainium2 kernel written in Bass

```python
import numpy as np
import jax
import jax.numpy as jnp

def _softmax(x, axis=-1):
    return jax.nn.softmax(x, axis=axis)

def _gelu(x):
    return jax.nn.gelu(x, approximate=True)

def _silu(x):
    return jax.nn.silu(x)

def _sigmoid(x):
    return jax.nn.sigmoid(x)

def _layernorm(x, axis=-1, eps=1e-05):
    m = jnp.mean(x, axis=axis, keepdims=True)
    v = jnp.var(x, axis=axis, keepdims=True)
    return (x - m) / jnp.sqrt(v + eps)

def _scatter_add(tgt, idx, src, axis=0):
    return tgt.at[idx].add(src)

def _segment_sum(src, seg, n):
    return jax.ops.segment_sum(src, seg, n)
kernel_name = 'mk_rec_standalone_d1_rec_r8_31b990'

def setup_inputs(seed: int=0):
    np.random.seed(seed)
    _w = jnp.asarray

    def _rec_inputs():
        import jax
        import jax.numpy as jnp
        _rk = jax.random.key(seed)
        r_numerical = 8.7408e-05 + 1.0001 * jax.random.normal(jax.random.fold_in(_rk, 1), (512, 13), jnp.float32)
        r_cat_features = jnp.stack([jax.random.randint(jax.random.fold_in(jax.random.fold_in(_rk, 2), 0), (512,), 2, 6250, jnp.int32), jax.random.randint(jax.random.fold_in(jax.random.fold_in(_rk, 2), 1), (512,), 0, 49998, jnp.int32), jax.random.randint(jax.random.fold_in(jax.random.fold_in(_rk, 2), 2), (512,), 0, 49999, jnp.int32), jax.random.randint(jax.random.fold_in(jax.random.fold_in(_rk, 2), 3), (512,), 0, 6250, jnp.int32), jax.random.randint(jax.random.fold_in(jax.random.fold_in(_rk, 2), 4), (512,), 0, 49999, jnp.int32), jax.random.randint(jax.random.fold_in(jax.random.fold_in(_rk, 2), 5), (512,), 0, 6250, jnp.int32), jax.random.randint(jax.random.fold_in(jax.random.fold_in(_rk, 2), 6), (512,), 0, 6250, jnp.int32), jax.random.randint(jax.random.fold_in(jax.random.fold_in(_rk, 2), 7), (512,), 1, 49998, jnp.int32), jax.random.randint(jax.random.fold_in(jax.random.fold_in(_rk, 2), 8), (512,), 0, 49991, jnp.int32), jax.random.randint(jax.random.fold_in(jax.random.fold_in(_rk, 2), 9), (512,), 0, 49998, jnp.int32), jax.random.randint(jax.random.fold_in(jax.random.fold_in(_rk, 2), 10), (512,), 2, 49999, jnp.int32), jax.random.randint(jax.random.fold_in(jax.random.fold_in(_rk, 2), 11), (512,), 1, 49998, jnp.int32), jax.random.randint(jax.random.fold_in(jax.random.fold_in(_rk, 2), 12), (512,), 0, 6250, jnp.int32), jax.random.randint(jax.random.fold_in(jax.random.fold_in(_rk, 2), 13), (512,), 2, 49998, jnp.int32), jax.random.randint(jax.random.fold_in(jax.random.fold_in(_rk, 2), 14), (512,), 1, 6250, jnp.int32), jax.random.randint(jax.random.fold_in(jax.random.fold_in(_rk, 2), 15), (512,), 0, 49998, jnp.int32), jax.random.randint(jax.random.fold_in(jax.random.fold_in(_rk, 2), 16), (512,), 0, 6250, jnp.int32), jax.random.randint(jax.random.fold_in(jax.random.fold_in(_rk, 2), 17), (512,), 0, 49997, jnp.int32), jax.random.randint(jax.random.fold_in(jax.random.fold_in(_rk, 2), 18), (512,), 1, 6250, jnp.int32), jax.random.randint(jax.random.fold_in(jax.random.fold_in(_rk, 2), 19), (512,), 1, 49996, jnp.int32), jax.random.randint(jax.random.fold_in(jax.random.fold_in(_rk, 2), 20), (512,), 0, 6250, jnp.int32), jax.random.randint(jax.random.fold_in(jax.random.fold_in(_rk, 2), 21), (512,), 2, 49998, jnp.int32), jax.random.randint(jax.random.fold_in(jax.random.fold_in(_rk, 2), 22), (512,), 0, 6250, jnp.int32), jax.random.randint(jax.random.fold_in(jax.random.fold_in(_rk, 2), 23), (512,), 0, 6250, jnp.int32), jax.random.randint(jax.random.fold_in(jax.random.fold_in(_rk, 2), 24), (512,), 2, 6250, jnp.int32), jax.random.randint(jax.random.fold_in(jax.random.fold_in(_rk, 2), 25), (512,), 0, 49999, jnp.int32)], axis=0)
        return (r_numerical, r_cat_features)
    r_numerical, r_cat_features = _rec_inputs()

    def _L0_rec_setup():
        import jax, jax.numpy as jnp
        import numpy as np
        B, T, V, D, NN = (4096, 26, 6250, 128, 13)
        HID = [256, 128, 1]

        def _glorot(key, shape):
            fan_in, fan_out = (shape[0], shape[1])
            std = np.sqrt(2.0 / (fan_in + fan_out))
            return jax.random.normal(key, shape, jnp.float32) * std
        key = jax.random.key(seed)
        ks = jax.random.split(key, 12)
        inp = {}
        inp['numerical'] = jax.random.normal(ks[0], (B, NN), jnp.float32)
        inp['cat_features'] = jax.random.randint(ks[1], (T, B), 0, V, dtype=jnp.int32)
        inp['tables'] = jax.random.normal(ks[2], (T, V, D), jnp.float32) * 0.01
        inp['w_wide'] = _glorot(ks[3], (NN, 1))
        inp['b_wide'] = jax.random.normal(ks[4], (1,), jnp.float32) * np.sqrt(1.0)
        din = NN + T * D
        inp['W1'] = _glorot(ks[5], (din, HID[0]))
        inp['b1'] = jax.random.normal(ks[6], (HID[0],), jnp.float32) * np.sqrt(1.0 / HID[0])
        inp['W2'] = _glorot(ks[7], (HID[0], HID[1]))
        inp['b2'] = jax.random.normal(ks[8], (HID[1],), jnp.float32) * np.sqrt(1.0 / HID[1])
        inp['W3'] = _glorot(ks[9], (HID[1], HID[2]))
        inp['b3'] = jax.random.normal(ks[10], (HID[2],), jnp.float32) * np.sqrt(1.0 / HID[2])
        return inp
    _L0_rec_all = _L0_rec_setup()
    _L0_rec_in = {k: v for k, v in _L0_rec_all.items() if k in ('tables', 'w_wide', 'b_wide', 'W1', 'b1', 'W2', 'b2', 'W3', 'b3')}
    del _L0_rec_all
    return {'r_numerical': r_numerical, 'r_cat_features': r_cat_features, 'L0_rec_tables': _L0_rec_in['tables'], 'L0_rec_w_wide': _L0_rec_in['w_wide'], 'L0_rec_b_wide': _L0_rec_in['b_wide'], 'L0_rec_W1': _L0_rec_in['W1'], 'L0_rec_b1': _L0_rec_in['b1'], 'L0_rec_W2': _L0_rec_in['W2'], 'L0_rec_b2': _L0_rec_in['b2'], 'L0_rec_W3': _L0_rec_in['W3'], 'L0_rec_b3': _L0_rec_in['b3']}

def reference(r_numerical, r_cat_features, L0_rec_tables, L0_rec_w_wide, L0_rec_b_wide, L0_rec_W1, L0_rec_b1, L0_rec_W2, L0_rec_b2, L0_rec_W3, L0_rec_b3):
    import jax
    import jax.numpy as jnp

    def _L0_rec_ref(numerical, cat_features, tables, w_wide, b_wide, W1, b1, W2, b2, W3, b3):
        import jax, jax.numpy as jnp
        import numpy as np
        B, T, V, D, NN = (4096, 26, 6250, 128, 13)
        HID = [256, 128, 1]

        def _glorot(key, shape):
            fan_in, fan_out = (shape[0], shape[1])
            std = np.sqrt(2.0 / (fan_in + fan_out))
            return jax.random.normal(key, shape, jnp.float32) * std
        emb = jax.vmap(lambda tab, idx: tab[idx])(tables, cat_features)
        emb_btd = jnp.transpose(emb, (1, 0, 2))
        wide_num = jax.nn.relu(numerical @ w_wide + b_wide)
        cat_sum = jnp.sum(emb_btd, axis=1)
        linear_output = cat_sum + wide_num
        x = jnp.concatenate([numerical, emb_btd.reshape(numerical.shape[0], T * D)], axis=1)
        x = jax.nn.relu(x @ W1 + b1)
        x = jax.nn.relu(x @ W2 + b2)
        dnn_output = x @ W3 + b3
        return jax.nn.sigmoid(dnn_output + linear_output)
    y = _L0_rec_ref(r_numerical, r_cat_features, L0_rec_tables, L0_rec_w_wide, L0_rec_b_wide, L0_rec_W1, L0_rec_b1, L0_rec_W2, L0_rec_b2, L0_rec_W3, L0_rec_b3)
    return y

_drawn_inputs = setup_inputs


def setup_inputs(seed=0):
    import zlib

    import numpy as np

    out = dict(_drawn_inputs(seed))
    spreads = {}
    factors = {'L0_rec_b1': 3.356, 'L0_rec_b2': 3.5}
    for name, (base, spread) in spreads.items():
        noise = np.random.default_rng([zlib.crc32(name.encode()), seed]).standard_normal(out[name].shape)
        drawn = base * np.exp(spread * noise) if base else spread * noise
        out[name] = jnp.asarray(drawn.astype(out[name].dtype))
    for name, factor in factors.items():
        out[name] = (out[name] * factor).astype(out[name].dtype)
    return out
```

```python
from contextlib import ExitStack

import concourse.bass as bass
from concourse import mybir

F32 = mybir.dt.float32
I32 = mybir.dt.int32
U32 = mybir.dt.uint32
ALU = mybir.AluOpType
ACT = mybir.ActivationFunctionType

P = 128
GROUP = 2
HALVES = 2


def build(nc, num, cat, tables, w_wide, b_wide, W1, b1, W2, b2, W3, b3, out):
    B, NUM = num.shape
    T, V, D = tables.shape
    H1, H2 = W2.shape
    CH = B // P
    STEPS = T // GROUP
    KH = H1 // P
    K0 = NUM + 1
    NW = H1 + D
    TILES = CH * GROUP
    CPH = CH // HALVES
    assert B == CH * P and D == P and T == STEPS * GROUP and H2 == P and T * CH <= P

    rows = tables.rearrange("t v d -> (t v) d")
    w1_rows = W1[NUM:NUM + T * D, :].rearrange("(t d) n -> d t n", d=D)

    ctx = ExitStack()
    with ctx:
        def sb(name, shape, dt=F32):
            return ctx.enter_context(nc.sbuf_tensor(name, shape, dt))

        def bank(name):
            return ctx.enter_context(nc.psum_tensor(name, [P, 512], F32))

        def sem(name):
            return ctx.enter_context(nc.semaphore(name))

        cat_sb = sb("cat_sb", [T * CH, P], I32)
        wrap = sb("wrap", [T * CH, P])
        wrapped = sb("wrapped", [T * CH, P])
        clamped = sb("clamped", [T * CH, P])
        base_i = sb("base_i", [P, T, CH], I32)
        base = sb("base", [P, T, CH])
        row_idx = sb("row_idx", [P, T * CH], I32)
        staged = sb("staged", [P, GROUP * CH], I32)

        ident = sb("ident", [P, P])
        w1 = sb("w1", [P, T, NW])
        w1_num = sb("w1_num", [K0, NW])
        w_wide_sb = sb("w_wide_sb", [K0, 1])
        w2 = sb("w2", [P, KH, H2])
        b2_sb = sb("b2_sb", [H2, 1])
        w3 = sb("w3", [H2, 1])
        b3_sb = sb("b3_sb", [P, 1])
        table_warm = sb("table_warm", [1, 1])

        num_sb = sb("num_sb", [P, CH, K0])
        num_t = sb("num_t", [K0, CH, P])
        wide = sb("wide", [P, CH])
        emb = sb("emb", [P, CH, GROUP, D])
        emb_t = sb("emb_t", [P, CH, GROUP, P])
        h1 = sb("h1", [P, CH, H1])
        h1_t = sb("h1_t", [P, CH, KH, P])
        h2_t = sb("h2_t", [H2, CH, P])
        logit = sb("logit", [P, CH])
        y = sb("y", [P, CH, D])

        acc = [bank(f"acc{c}") for c in range(CH)]
        turn = [bank(f"turn{i}") for i in range(2)]
        hid = bank("hid")
        deep = bank("deep")

        cat_loaded = sem("cat_loaded")
        num_loaded = sem("num_loaded")
        small_loaded = sem("small_loaded")
        w2_loaded = sem("w2_loaded")
        w1_loaded = sem("w1_loaded")
        consts = sem("consts")
        index_steps = sem("index_steps")
        index_turned = sem("index_turned")
        rows_ready = sem("rows_ready")
        padded = sem("padded")
        idents = sem("idents")
        num_turned = sem("num_turned")
        num_copied = sem("num_copied")
        wide_done = sem("wide_done")
        wide_ready = sem("wide_ready")
        staged_ready = [sem(f"staged_ready{h}") for h in range(HALVES)]
        slot_free = sem("slot_free")
        gathered = [sem(f"gathered{c}") for c in range(CH)]
        turned = [sem(f"turned{c}") for c in range(CH)]
        copied = [sem(f"copied{c}") for c in range(CH)]
        used = [sem(f"used{c}") for c in range(CH)]
        summed = sem("summed")
        h1_ready = sem("h1_ready")
        h1_turned = sem("h1_turned")
        h1_copied = sem("h1_copied")
        h2_done = sem("h2_done")
        h2_ready = sem("h2_ready")
        dnn_done = sem("dnn_done")
        logit_ready = sem("logit_ready")
        y_ready = sem("y_ready")
        stored = sem("stored")

        SMALL = 7
        W1_PARTS = 13

        block = ctx.enter_context(nc.Block())

        @block.sync
        def _(sp):
            sp.dma_start(cat_sb[:, :], cat.rearrange("t (c p) -> (t c) p", p=P)).then_inc(cat_loaded, 16)
            sp.wait_ge(padded, 3)
            sp.dma_start(num_sb[:, :, 0:NUM], num.rearrange("(c p) k -> p c k", p=P)).then_inc(num_loaded, 16)
            sp.dma_start(w1_num[0:NUM, 0:H1], W1[0:NUM, :]).then_inc(small_loaded, 16)
            sp.dma_start(w1_num[NUM:K0, 0:H1], b1.unsqueeze(0)).then_inc(small_loaded, 16)
            sp.dma_start(w_wide_sb[0:NUM, :], w_wide).then_inc(small_loaded, 16)
            sp.dma_start(w_wide_sb[NUM:K0, :], b_wide.unsqueeze(0)).then_inc(small_loaded, 16)
            sp.dma_start(b2_sb[:, :], b2.unsqueeze(1)).then_inc(small_loaded, 16)
            sp.dma_start(w3[:, :], W3).then_inc(small_loaded, 16)
            sp.dma_start(b3_sb[:, :], b3.partition_broadcast(P)).then_inc(small_loaded, 16)
            sp.dma_start(w2[:, :, :], W2.rearrange("(k p) n -> p k n", p=P)).then_inc(w2_loaded, 16)
            for c in range(CH):
                sp.wait_ge(y_ready, c + 1)
                sp.dma_start(out[c * P:(c + 1) * P, :], y[:, c, :]).then_inc(stored, 16)
            sp.wait_ge(stored, 16 * CH)

        @block.gpsimd
        def _(gp):
            nc.gpsimd.memset(ident[:, :], 0.0).then_inc(consts, 1)
            gp.wait_ge(consts, 1)
            nc.gpsimd.affine_select(out=ident[:, :], in_=ident[:, :], compare_op=ALU.not_equal, fill=1.0,
                                    base=0, pattern=[[-1, P]], channel_multiplier=1).then_inc(consts, 1)
            nc.gpsimd.iota(base_i[:, :, :], pattern=[[V, T], [0, CH]], base=0,
                           channel_multiplier=0).then_inc(consts, 1)

            def gathers(step, first=False):
                for c in range(CH):
                    half = c // CPH
                    if c % CPH == 0:
                        gp.wait_ge(staged_ready[half], step + 1)
                    if not first:
                        gp.wait_ge(turned[c], step)
                        gp.sem_inc(slot_free, 1)
                    for g in range(GROUP):
                        nc.gpsimd.indirect_dma_start(
                            emb[:, c, g, :], None, rows,
                            bass.IndirectOffsetOnAxis(ap=staged[:, c * GROUP + g:c * GROUP + g + 1], axis=0),
                        ).then_inc(gathered[c], 16)

            gathers(0, first=True)
            with gp.Fori(1, STEPS) as step:
                gathers(step)

        @block.tensor
        def _(pe):
            def turn_group(step, c, first=False):
                pe.wait_ge(gathered[c], 16 * GROUP * (step + 1))
                if c >= 2:
                    pe.wait_ge(copied[c - 2], step + 1)
                elif not first:
                    pe.wait_ge(copied[c + 2], step)
                for g in range(GROUP):
                    mm = nc.tensor.transpose(turn[c % 2][:, g * P:(g + 1) * P], emb[:, c, g, :], ident[:, :])
                mm.then_inc(turned[c], 1)

            def sum_group(step, c, last=False):
                pe.wait_ge(copied[c], step + 1)
                for g in range(GROUP):
                    mm = nc.tensor.matmul(acc[c][:, 0:NW], emb_t[:, c, g, :],
                                          w1[:, GROUP * step + g, :], start=False, stop=last and g == GROUP - 1)
                mm.then_inc(used[c], 1)

            pe.wait_ge(consts, 2)
            pe.wait_ge(index_steps, 3)
            nc.tensor.transpose(hid[:, 0:T * CH], clamped[:, :], ident[0:T * CH, 0:T * CH]).then_inc(index_turned, 1)
            pe.wait_ge(num_loaded, 16)
            for c in range(CH):
                mm = nc.tensor.transpose(deep[0:K0, c * P:(c + 1) * P], num_sb[:, c, :], ident[:, :])
            mm.then_inc(num_turned, 1)
            pe.wait_ge(num_copied, 1)
            pe.wait_ge(small_loaded, 16 * SMALL)
            for c in range(CH):
                nc.tensor.matmul(acc[c][:, 0:NW], num_t[:, c, :], w1_num[:, :], start=True, stop=False)
            for c in range(CH):
                mm = nc.tensor.matmul(turn[1][:, c:c + 1], num_t[:, c, :], w_wide_sb[:, :], start=True, stop=True)
            mm.then_inc(wide_done, 1)
            pe.wait_ge(wide_ready, 1)

            turn_group(0, 0, first=True)
            pe.wait_ge(idents, 1)
            pe.wait_ge(w1_loaded, 16 * W1_PARTS)

            def whole_step(step, first=False):
                for c in range(CH):
                    if c < CH - 1:
                        turn_group(step, c + 1, first=first)
                    else:
                        turn_group(step + 1, 0)
                    sum_group(step, c)

            whole_step(0, first=True)
            with pe.Fori(1, STEPS - 1) as step:
                whole_step(step)

            last = STEPS - 1

            def turn_h1(c):
                pe.wait_ge(h1_ready, c + 1)
                if c >= 1:
                    pe.wait_ge(h1_copied, c)
                for k in range(KH):
                    mm = nc.tensor.transpose(hid[:, k * P:(k + 1) * P], h1[:, c, k * P:(k + 1) * P], ident[:, :])
                mm.then_inc(h1_turned, 1)

            def layer2(c):
                pe.wait_ge(h1_copied, c + 1)
                if c == 0:
                    pe.wait_ge(w2_loaded, 16)
                if c >= 1:
                    pe.wait_ge(h2_ready, c)
                for k in range(KH):
                    mm = nc.tensor.matmul(deep[:, 0:P], w2[:, k, :], h1_t[:, c, k, :],
                                          start=(k == 0), stop=(k == KH - 1))
                mm.then_inc(h2_done, 1)

            def layer3(c):
                pe.wait_ge(h2_ready, c + 1)
                if c >= 1:
                    pe.wait_ge(logit_ready, c)
                nc.tensor.matmul(hid[:, 256 + c:257 + c], h2_t[:, c, :], w3[:, :],
                                 start=True, stop=True).then_inc(dnn_done, 1)

            for c in range(CH):
                if c < CH - 1:
                    turn_group(last, c + 1)
                sum_group(last, c, last=True)
                turn_h1(c)
                layer2(c)
                layer3(c)

        @block.vector
        def _(dve):
            nc.vector.memset(w1_num[:, H1:NW], 0.0).then_inc(padded, 1)
            nc.vector.memset(num_sb[:, :, NUM:K0], 1.0).then_inc(padded, 1)
            nc.vector.memset(b3_sb[:, :], 0.0).then_inc(padded, 1)
            dve.wait_ge(cat_loaded, 16)
            nc.vector.tensor_scalar(wrap[:, :], cat_sb[:, :], 0.0, float(V), ALU.is_lt, ALU.mult).then_inc(index_steps, 1)
            dve.wait_ge(index_steps, 1)
            nc.vector.tensor_tensor(wrapped[:, :], wrap[:, :], cat_sb[:, :], ALU.add).then_inc(index_steps, 1)
            dve.wait_ge(index_steps, 2)
            nc.vector.tensor_scalar(clamped[:, :], wrapped[:, :], 0.0, float(V - 1), ALU.max, ALU.min).then_inc(index_steps, 1)
            dve.wait_ge(consts, 3)
            nc.vector.tensor_copy(base[:, :, :], base_i[:, :, :]).then_inc(index_steps, 1)
            dve.wait_ge(index_steps, 4)
            dve.wait_ge(index_turned, 1)
            nc.vector.tensor_tensor(row_idx[:, :], hid[:, 0:T * CH], base[:, :, :].rearrange("p t c -> p (t c)"),
                                    ALU.add).then_inc(rows_ready, 1)
            dve.wait_ge(rows_ready, 1)

            by_step = row_idx[:, :].rearrange("p (s g c) -> p s c g", g=GROUP, c=CH)
            slots = staged[:, :].rearrange("p (c g) -> p c g", g=GROUP)

            def stage(step, half, first=False):
                if not first:
                    for c in range(half * CPH, (half + 1) * CPH):
                        dve.wait_ge(gathered[c], 16 * GROUP * step)
                src = row_idx[:, :].rearrange("p (s g c) -> p s c g", g=GROUP, c=CH)
                nc.vector.tensor_copy(slots[:, half * CPH:(half + 1) * CPH, :],
                                      src[:, bass.ds(step, 1), half * CPH:(half + 1) * CPH, :].squeeze(1)
                                      ).then_inc(staged_ready[half], 1)

            def copy_out(step, c, first=False):
                dve.wait_ge(turned[c], step + 1)
                if not first:
                    dve.wait_ge(used[c], step)
                nc.vector.tensor_copy(emb_t[:, c, :, :].rearrange("p g n -> p (g n)"),
                                      turn[c % 2][:, 0:GROUP * P]).then_inc(copied[c], 1)

            for half in range(HALVES):
                stage(0, half, first=True)
            dve.wait_ge(num_turned, 1)
            nc.vector.tensor_copy(num_t[:, :, :].rearrange("k c p -> k (c p)"), deep[0:K0, 0:CH * P]).then_inc(num_copied, 1)
            dve.wait_ge(wide_done, 1)
            nc.vector.tensor_scalar(wide[:, :], turn[1][:, 0:CH], 0.0, b3_sb[:, 0:1], ALU.max, ALU.add).then_inc(wide_ready, 1)
            for c in range(CH):
                copy_out(0, c, first=True)
                if c % CPH == CPH - 1:
                    stage(1, c // CPH)
            with dve.Fori(1, STEPS - 1) as step:
                for c in range(CH):
                    copy_out(step, c)
                    if c % CPH == CPH - 1:
                        stage(step + 1, c // CPH)
            last = STEPS - 1

            def tail(c):
                dve.wait_ge(used[c], STEPS)
                nc.vector.tensor_scalar(h1[:, c, :], acc[c][:, 0:H1], 0.0, None, ALU.max).then_inc(h1_ready, 1)
                dve.wait_ge(h1_turned, c + 1)
                nc.vector.tensor_copy(h1_t[:, c, :, :].rearrange("p k n -> p (k n)"), hid[:, 0:KH * P]).then_inc(h1_copied, 1)
                dve.wait_ge(h2_done, c + 1)
                nc.vector.tensor_scalar(h2_t[:, c, :], deep[:, 0:P], b2_sb[:, 0:1], 0.0, ALU.add, ALU.max).then_inc(h2_ready, 1)
                dve.wait_ge(dnn_done, c + 1)
                nc.vector.tensor_tensor(logit[:, c:c + 1], hid[:, 256 + c:257 + c], wide[:, c:c + 1], ALU.add).then_inc(logit_ready, 1)

            copy_out(last, 0)
            for c in range(CH):
                if c < CH - 1:
                    copy_out(last, c + 1)
                tail(c)

        @block.scalar
        def _(act):
            per = T // W1_PARTS
            for i in range(W1_PARTS):
                act.dma_start(w1[:, i * per:(i + 1) * per, 0:H1], w1_rows[:, i * per:(i + 1) * per, :]).then_inc(w1_loaded, 16)
            act.wait_ge(consts, 2)
            nc.scalar.activation(table_warm[:, :], ident[0:1, 0:1], ACT.Sigmoid)
            nc.scalar.activation(w1[:, :, H1:NW], ident[:, :].unsqueeze(1).broadcast_to([P, T, P]), ACT.Copy).then_inc(idents, 1)
            for c in range(CH):
                act.wait_ge(logit_ready, c + 1)
                nc.scalar.activation(y[:, c, :], acc[c][:, H1:NW], ACT.Sigmoid, bias=logit[:, c:c + 1]).then_inc(y_ready, 1)


_NAMES = ["r_numerical", "r_cat_features", "L0_rec_tables", "L0_rec_w_wide", "L0_rec_b_wide", "L0_rec_W1",
          "L0_rec_b1", "L0_rec_W2", "L0_rec_b2", "L0_rec_W3", "L0_rec_b3"]


def kernel(**inputs):
    import numpy as np
    import concourse.bacc as bacc
    from concourse import mybir
    from concourse.bass_utils import run_bass_kernel_spmd

    nc = bacc.Bacc("TRN2", target_bir_lowering=False, num_devices=1)
    arrays, args = {}, []
    for name in _NAMES:
        a = np.ascontiguousarray(inputs[name])
        arrays[f"in_{name}"] = a
        args.append(nc.dram_tensor(f"in_{name}", a.shape, mybir.dt.from_np(a.dtype), kind="ExternalInput").ap())
    shape = (inputs["r_numerical"].shape[0], inputs["L0_rec_tables"].shape[2])
    args.append(nc.dram_tensor("out", shape, mybir.dt.float32, kind="ExternalOutput").ap())
    build(nc, *args)
    result = run_bass_kernel_spmd(nc, [arrays], core_ids=[0])
    return result.results[0]["out"]
```

```python
from contextlib import ExitStack

import concourse.bass as bass
from concourse import mybir

F32 = mybir.dt.float32
I32 = mybir.dt.int32
ALU = mybir.AluOpType
ACT = mybir.ActivationFunctionType

P = 128
PAIR = 2


def build(nc, num, cat, tables, w_wide, b_wide, W1, b1, W2, b2, W3, b3, out):
    B, NUM = num.shape
    T, V, D = tables.shape
    H1, H2 = W2.shape
    CH = B // P
    STEPS = T // PAIR
    LAST = STEPS - 1
    KH = H1 // P
    K0 = NUM + 1
    TABLE_DONE = 16 * CH
    assert B == CH * P and D == P and T == STEPS * PAIR and H2 == P and KH == 2 and T * CH <= P

    rows = tables.rearrange("t v d -> (t v) d")

    ctx = ExitStack()
    with ctx:
        def sb(name, shape, dt=F32):
            return ctx.enter_context(nc.sbuf_tensor(name, shape, dt))

        def bank(name):
            return ctx.enter_context(nc.psum_tensor(name, [P, 512], F32))

        def sem(name):
            return ctx.enter_context(nc.semaphore(name))

        def pair_of_sems(name):
            return [sem(f"{name}{par}") for par in range(PAIR)]

        def chunk(c):
            return slice(c * P, (c + 1) * P)

        cat_sb = sb("cat_sb", [T * CH, P], I32)
        wrap = sb("wrap", [T * CH, P])
        wrapped = sb("wrapped", [T * CH, P])
        clamped = sb("clamped", [T * CH, P])
        base_i = sb("base_i", [P, T, CH], I32)
        base = sb("base", [P, T, CH])
        row_idx = sb("row_idx", [P, T * CH], I32)
        staged = sb("staged", [P, PAIR, CH], I32)

        ident = sb("ident", [P, P])
        w1 = sb("w1", [P, PAIR, H1])
        w1_num = sb("w1_num", [NUM, H1])
        vec_rows = sb("vec_rows", [KH + 2, P])
        vec_cols = sb("vec_cols", [P, KH + 2])
        b1_col, b2_col, w3_col = vec_cols[:, 0:KH], vec_cols[:, KH:KH + 1], vec_cols[:, KH + 1:KH + 2]
        w_wide_sb = sb("w_wide_sb", [K0, 1])
        w2 = sb("w2", [P, KH, H2])
        b3_sb = sb("b3_sb", [P, 1])
        table_warm = sb("table_warm", [1, 1])

        num_sb = sb("num_sb", [P, CH, K0])
        num_t = sb("num_t", [K0, B])
        wide = sb("wide", [P, CH])
        emb = sb("emb", [P, PAIR, CH, D])
        emb_t = sb("emb_t", [P, PAIR, B])
        emb_sum = sb("emb_sum", [P, B])
        h1 = sb("h1", [P, KH, B])
        h2 = sb("h2", [H2, B])
        logit = sb("logit", [P, CH])
        y = sb("y", [P, CH, D])

        first_layer = [bank(f"first_layer{k}") for k in range(KH)]
        turn = [bank(f"turn{par}") for par in range(PAIR)]
        deep = bank("deep")
        sum_turned = [bank(f"sum_turned{i}") for i in range(2)]
        scalars = bank("scalars")

        cat_loaded = sem("cat_loaded")
        num_loaded = sem("num_loaded")
        small_loaded = sem("small_loaded")
        w1_loaded = pair_of_sems("w1_loaded")
        ident_steps = sem("ident_steps")
        base_ready = sem("base_ready")
        ones_ready = sem("ones_ready")
        vecs_ready = sem("vecs_ready")
        index_steps = sem("index_steps")
        index_turned = sem("index_turned")
        rows_ready = sem("rows_ready")
        staged_ready = pair_of_sems("staged_ready")
        num_turned = sem("num_turned")
        num_copied = sem("num_copied")
        scalars_done = sem("scalars_done")
        wide_ready = sem("wide_ready")
        slot_free = sem("slot_free")
        gathered = pair_of_sems("gathered")
        turned = pair_of_sems("turned")
        copied = pair_of_sems("copied")
        added = pair_of_sems("added")
        used = pair_of_sems("used")
        tail_gathered = [sem(f"tail_gathered{c}") for c in range(CH)]
        tail_turned = sem("tail_turned")
        tail_copied = sem("tail_copied")
        tail_added = sem("tail_added")
        h1_done = sem("h1_done")
        h1_low_ready = sem("h1_low_ready")
        h1_high_ready = sem("h1_high_ready")
        h2_done = sem("h2_done")
        h2_ready = sem("h2_ready")
        dnn_done = sem("dnn_done")
        logit_ready = sem("logit_ready")
        sum_done = sem("sum_done")
        y_ready = sem("y_ready")
        stored = sem("stored")

        SMALL = 8

        block = ctx.enter_context(nc.Block())

        @block.sync
        def _(sp):
            sp.dma_start(cat_sb[:, :], cat.rearrange("t (c p) -> (t c) p", p=P)).then_inc(cat_loaded, 16)

            def load_w1(step, par, first=False):
                if not first:
                    sp.wait_ge(used[par], step)
                sp.dma_start(w1[:, par, :], W1[bass.ds(NUM + (step * PAIR + par) * D, D), :]
                             ).then_inc(w1_loaded[par], 16)

            for par in range(PAIR):
                load_w1(0, par, first=True)
            with sp.Fori(1, STEPS) as step:
                for par in range(PAIR):
                    load_w1(step, par)

            for c in range(CH):
                sp.wait_ge(y_ready, c + 1)
                sp.dma_start(out[chunk(c), :], y[:, c, :]).then_inc(stored, 16)
            sp.wait_ge(stored, 16 * CH)

        @block.gpsimd
        def _(gp):
            nc.gpsimd.memset(ident[:, :], 0.0).then_inc(ident_steps, 1)
            gp.wait_ge(ident_steps, 1)
            nc.gpsimd.affine_select(out=ident[:, :], in_=ident[:, :], compare_op=ALU.not_equal, fill=1.0,
                                    base=0, pattern=[[-1, P]], channel_multiplier=1).then_inc(ident_steps, 1)
            nc.gpsimd.iota(base_i[:, :, :], pattern=[[V, T], [0, CH]], base=0,
                           channel_multiplier=0).then_inc(base_ready, 1)

            def gather(step, par, first=False, tail=False):
                if first:
                    gp.wait_ge(staged_ready[0], 1)
                else:
                    gp.wait_ge(staged_ready[par], step + 1 - par)
                if not first:
                    gp.wait_ge(turned[par], step)
                    gp.sem_inc(slot_free, 1)
                for c in range(CH):
                    nc.gpsimd.indirect_dma_start(
                        emb[:, par, c, :], None, rows,
                        bass.IndirectOffsetOnAxis(ap=staged[:, par, c:c + 1], axis=0),
                    ).then_inc(tail_gathered[c] if tail else gathered[par], 16)

            for par in range(PAIR):
                gather(0, par, first=True)
            with gp.Fori(1, LAST) as step:
                for par in range(PAIR):
                    gather(step, par)
            gather(LAST, 0)
            gather(LAST, 1, tail=True)

        @block.tensor
        def _(pe):
            pe.wait_ge(ident_steps, 2)
            pe.wait_ge(index_steps, 3)
            nc.tensor.transpose(sum_turned[0][:, 0:T * CH], clamped[:, :],
                                ident[0:T * CH, 0:T * CH]).then_inc(index_turned, 1)
            pe.wait_ge(num_loaded, 16)
            pe.wait_ge(ones_ready, 1)
            for c in range(CH):
                mm = nc.tensor.transpose(deep[0:K0, chunk(c)], num_sb[:, c, :], ident[:, :])
            mm.then_inc(num_turned, 1)
            pe.wait_ge(num_copied, 1)
            pe.wait_ge(small_loaded, 16 * SMALL)
            for k in range(KH):
                nc.tensor.matmul(first_layer[k][:, :], w1_num[:, chunk(k)], num_t[0:NUM, :], start=True, stop=True)
            for c in range(CH):
                nc.tensor.matmul(scalars[:, CH + c:CH + c + 1], num_t[:, chunk(c)], w_wide_sb[:, :],
                                 start=True, stop=True)
            nc.tensor.transpose(scalars[:, 2 * CH:2 * CH + KH + 2], vec_rows[:, :], ident[0:KH + 2, 0:KH + 2]
                                ).then_inc(scalars_done, 1)

            def turn_table(step, par, first=False):
                pe.wait_ge(gathered[par], TABLE_DONE * (step + 1))
                if not first:
                    pe.wait_ge(added[par], step)
                for c in range(CH):
                    mm = nc.tensor.transpose(turn[par][:, chunk(c)], emb[:, par, c, :], ident[:, :])
                mm.then_inc(turned[par], 1)

            def sum_table(step, par):
                pe.wait_ge(w1_loaded[par], 16 * (step + 1))
                pe.wait_ge(copied[par], step + 1)
                for k in range(KH):
                    mm = nc.tensor.matmul(first_layer[k][:, :], w1[:, par, chunk(k)], emb_t[:, par, :],
                                          start=False, stop=False, skip_group_check=True)
                mm.then_inc(used[par], 1)

            turn_table(0, 0, first=True)
            turn_table(0, 1, first=True)
            sum_table(0, 0)
            turn_table(1, 0)
            sum_table(0, 1)
            with pe.Fori(1, LAST) as step:
                turn_table(step, 1)
                sum_table(step, 0)
                turn_table(step + 1, 0)
                sum_table(step, 1)

            def turn_chunk(c):
                pe.wait_ge(tail_gathered[c], 16)
                if c < 2:
                    pe.wait_ge(added[(c + 1) % 2], LAST + c)
                else:
                    pe.wait_ge(tail_added, c - 1)
                nc.tensor.transpose(turn[(c + 1) % 2][:, 0:P], emb[:, 1, c, :], ident[:, :]).then_inc(tail_turned, 1)

            def sum_chunk(c):
                if c == 0:
                    pe.wait_ge(w1_loaded[1], 16 * STEPS)
                else:
                    pe.wait_ge(h1_low_ready, c)
                    pe.wait_ge(h1_high_ready, c)
                pe.wait_ge(tail_copied, c + 1)
                for k in range(KH):
                    mm = nc.tensor.matmul(first_layer[k][:, chunk(c)], w1[:, 1, chunk(k)], emb_t[:, 1, chunk(c)],
                                          start=False, stop=False, skip_group_check=True)
                mm.then_inc(h1_done, 1)

            def layer2(c):
                pe.wait_ge(h1_low_ready, c + 1)
                pe.wait_ge(h1_high_ready, c + 1)
                if c >= 1:
                    pe.wait_ge(h2_ready, c)
                for k in range(KH):
                    mm = nc.tensor.matmul(deep[:, chunk(c)], w2[:, k, :], h1[:, k, chunk(c)],
                                          start=(k == 0), stop=(k == KH - 1))
                mm.then_inc(h2_done, 1)

            def layer3(c):
                pe.wait_ge(h2_ready, c + 1)
                if c == 0:
                    pe.wait_ge(vecs_ready, 1)
                else:
                    pe.wait_ge(logit_ready, c)
                nc.tensor.matmul(scalars[:, c:c + 1], h2[:, chunk(c)], w3_col, start=True, stop=True
                                 ).then_inc(dnn_done, 1)

            def turn_sum(c):
                pe.wait_ge(tail_added, c + 1)
                if c >= 2:
                    pe.wait_ge(y_ready, c - 1)
                nc.tensor.transpose(sum_turned[c % 2][:, 0:P], emb_sum[:, chunk(c)], ident[:, :]).then_inc(sum_done, 1)

            sum_table(LAST, 0)
            turn_chunk(0)
            sum_chunk(0)
            for c in range(CH - 1):
                turn_chunk(c + 1)
                layer2(c)
                sum_chunk(c + 1)
                layer3(c)
                turn_sum(c)
            turn_sum(CH - 1)
            layer2(CH - 1)
            layer3(CH - 1)

        @block.vector
        def _(dve):
            nc.vector.memset(num_sb[:, :, NUM:K0], 1.0).then_inc(ones_ready, 1)
            dve.wait_ge(cat_loaded, 16)
            nc.vector.tensor_scalar(wrap[:, :], cat_sb[:, :], 0.0, float(V), ALU.is_lt, ALU.mult
                                    ).then_inc(index_steps, 1)
            dve.wait_ge(index_steps, 1)
            nc.vector.tensor_tensor(wrapped[:, :], wrap[:, :], cat_sb[:, :], ALU.add).then_inc(index_steps, 1)
            dve.wait_ge(index_steps, 2)
            nc.vector.tensor_scalar(clamped[:, :], wrapped[:, :], 0.0, float(V - 1), ALU.max, ALU.min
                                    ).then_inc(index_steps, 1)
            dve.wait_ge(base_ready, 1)
            nc.vector.tensor_copy(base[:, :, :], base_i[:, :, :]).then_inc(index_steps, 1)
            dve.wait_ge(index_steps, 4)
            dve.wait_ge(index_turned, 1)
            nc.vector.tensor_tensor(staged[:, :, :].rearrange("p t c -> p (t c)"), sum_turned[0][:, 0:PAIR * CH],
                                    base[:, 0:PAIR, :].rearrange("p t c -> p (t c)"), ALU.add
                                    ).then_inc(staged_ready[0], 1)
            nc.vector.tensor_tensor(row_idx[:, :], sum_turned[0][:, 0:T * CH],
                                    base[:, :, :].rearrange("p t c -> p (t c)"), ALU.add).then_inc(rows_ready, 1)

            def stage(step, par, first=False):
                if first:
                    dve.wait_ge(rows_ready, 1)
                dve.wait_ge(gathered[par], TABLE_DONE * step)
                nc.vector.tensor_copy(staged[:, par, :], row_idx[:, bass.ds((step * PAIR + par) * CH, CH)]
                                      ).then_inc(staged_ready[par], 1)

            def add_table(step, par, first=False):
                dve.wait_ge(copied[par], step + 1)
                if first:
                    nc.vector.tensor_copy(emb_sum[:, :], turn[par][:, :]).then_inc(added[par], 1)
                    return
                dve.wait_ge(added[1 - par], step + par)
                nc.vector.tensor_tensor(emb_sum[:, :], turn[par][:, :], emb_sum[:, :], ALU.add
                                        ).then_inc(added[par], 1)

            dve.wait_ge(num_turned, 1)
            nc.vector.tensor_copy(num_t[:, :], deep[0:K0, :]).then_inc(num_copied, 1)
            dve.wait_ge(scalars_done, 1)
            dve.wait_ge(small_loaded, 16 * SMALL)
            nc.vector.tensor_scalar(wide[:, :], scalars[:, CH:2 * CH], 0.0, b3_sb[:, 0:1], ALU.max, ALU.add
                                    ).then_inc(wide_ready, 1)
            nc.vector.tensor_copy(vec_cols[:, :], scalars[:, 2 * CH:2 * CH + KH + 2]).then_inc(vecs_ready, 1)

            for par in range(PAIR):
                stage(1, par, first=True)
                add_table(0, par, first=(par == 0))
            with dve.Fori(1, LAST) as step:
                for par in range(PAIR):
                    stage(step + 1, par)
                    add_table(step, par)
            add_table(LAST, 0)

            def add_chunk(c):
                dve.wait_ge(tail_copied, c + 1)
                if c == 0:
                    dve.wait_ge(added[0], STEPS)
                nc.vector.tensor_tensor(emb_sum[:, chunk(c)], turn[(c + 1) % 2][:, 0:P], emb_sum[:, chunk(c)], ALU.add
                                        ).then_inc(tail_added, 1)

            def relu_h1_high(c):
                dve.wait_ge(h1_done, c + 1)
                if c == 0:
                    dve.wait_ge(vecs_ready, 1)
                nc.vector.tensor_scalar(h1[:, 1, chunk(c)], first_layer[1][:, chunk(c)], b1_col[:, 1:2], 0.0,
                                        ALU.add, ALU.max).then_inc(h1_high_ready, 1)

            def relu_h2(c):
                dve.wait_ge(h2_done, c + 1)
                nc.vector.tensor_scalar(h2[:, chunk(c)], deep[:, chunk(c)], b2_col, 0.0, ALU.add, ALU.max
                                        ).then_inc(h2_ready, 1)

            def add_wide(c):
                dve.wait_ge(dnn_done, c + 1)
                if c == 0:
                    dve.wait_ge(wide_ready, 1)
                nc.vector.tensor_tensor(logit[:, c:c + 1], scalars[:, c:c + 1], wide[:, c:c + 1], ALU.add
                                        ).then_inc(logit_ready, 1)

            add_chunk(0)
            relu_h1_high(0)
            for c in range(CH - 1):
                add_chunk(c + 1)
                relu_h2(c)
                relu_h1_high(c + 1)
                add_wide(c)
            relu_h2(CH - 1)
            add_wide(CH - 1)

        @block.scalar
        def _(act):
            act.wait_ge(ones_ready, 1)
            act.dma_start(num_sb[:, :, 0:NUM], num.rearrange("(c p) k -> p c k", p=P)).then_inc(num_loaded, 16)
            act.dma_start(w1_num[:, :], W1[0:NUM, :]).then_inc(small_loaded, 16)
            act.dma_start(w_wide_sb[0:NUM, :], w_wide).then_inc(small_loaded, 16)
            act.dma_start(w_wide_sb[NUM:K0, :], b_wide.unsqueeze(0)).then_inc(small_loaded, 16)
            act.dma_start(b3_sb[:, :], b3.partition_broadcast(P)).then_inc(small_loaded, 16)
            act.dma_start(vec_rows[0:KH, :], b1.rearrange("(k p) -> k p", p=P)).then_inc(small_loaded, 16)
            act.dma_start(vec_rows[KH:KH + 1, :], b2.unsqueeze(0)).then_inc(small_loaded, 16)
            act.dma_start(vec_rows[KH + 1:KH + 2, :], W3.rearrange("p a -> a p")).then_inc(small_loaded, 16)
            act.dma_start(w2[:, :, :], W2.rearrange("(k p) n -> p k n", p=P)).then_inc(small_loaded, 16)
            act.wait_ge(ident_steps, 2)
            nc.scalar.activation(table_warm[:, :], ident[0:1, 0:1], ACT.Sigmoid)

            def copy_table(step, par, first=False):
                act.wait_ge(turned[par], step + 1)
                if not first:
                    act.wait_ge(used[par], step)
                nc.scalar.copy(emb_t[:, par, :], turn[par][:, :]).then_inc(copied[par], 1)

            for par in range(PAIR):
                copy_table(0, par, first=True)
            with act.Fori(1, LAST) as step:
                for par in range(PAIR):
                    copy_table(step, par)
            copy_table(LAST, 0)

            def copy_chunk(c):
                act.wait_ge(tail_turned, c + 1)
                if c == 0:
                    act.wait_ge(used[1], LAST)
                nc.scalar.copy(emb_t[:, 1, chunk(c)], turn[(c + 1) % 2][:, 0:P]).then_inc(tail_copied, 1)

            def relu_h1_low(c):
                act.wait_ge(h1_done, c + 1)
                if c == 0:
                    act.wait_ge(vecs_ready, 1)
                nc.scalar.activation(h1[:, 0, chunk(c)], first_layer[0][:, chunk(c)], ACT.Relu,
                                     bias=b1_col[:, 0:1]).then_inc(h1_low_ready, 1)

            def squash(c):
                act.wait_ge(sum_done, c + 1)
                act.wait_ge(logit_ready, c + 1)
                nc.scalar.activation(y[:, c, :], sum_turned[c % 2][:, 0:P], ACT.Sigmoid,
                                     bias=logit[:, c:c + 1]).then_inc(y_ready, 1)

            copy_chunk(0)
            relu_h1_low(0)
            for c in range(CH - 1):
                copy_chunk(c + 1)
                relu_h1_low(c + 1)
                squash(c)
            squash(CH - 1)


_NAMES = ["r_numerical", "r_cat_features", "L0_rec_tables", "L0_rec_w_wide", "L0_rec_b_wide", "L0_rec_W1",
          "L0_rec_b1", "L0_rec_W2", "L0_rec_b2", "L0_rec_W3", "L0_rec_b3"]


def kernel(**inputs):
    import numpy as np
    import concourse.bacc as bacc
    from concourse import mybir
    from concourse.bass_utils import run_bass_kernel_spmd

    nc = bacc.Bacc("TRN2", target_bir_lowering=False, num_devices=1)
    arrays, args = {}, []
    for name in _NAMES:
        a = np.ascontiguousarray(inputs[name])
        arrays[f"in_{name}"] = a
        args.append(nc.dram_tensor(f"in_{name}", a.shape, mybir.dt.from_np(a.dtype), kind="ExternalInput").ap())
    shape = (inputs["r_numerical"].shape[0], inputs["L0_rec_tables"].shape[2])
    args.append(nc.dram_tensor("out", shape, mybir.dt.float32, kind="ExternalOutput").ap())
    build(nc, *args)
    result = run_bass_kernel_spmd(nc, [arrays], core_ids=[0])
    return result.results[0]["out"]
```

```python
from contextlib import ExitStack

import concourse.bass as bass
from concourse import mybir

F32 = mybir.dt.float32
I32 = mybir.dt.int32
ALU = mybir.AluOpType
ACT = mybir.ActivationFunctionType

P = 128
PAIR = 2


def build(nc, num, cat, tables, w_wide, b_wide, W1, b1, W2, b2, W3, b3, out):
    B, NUM = num.shape
    T, V, D = tables.shape
    H1, H2 = W2.shape
    CH = B // P
    STEPS = T // PAIR
    TAIL = STEPS - 1
    TILES = PAIR * CH
    KH = H1 // P
    K0 = NUM + 1
    TABLE_DONE = 16 * CH
    assert B == CH * P and D == P and T == STEPS * PAIR and H2 == P and KH == 2 and T * CH <= P

    rows = tables.rearrange("t v d -> (t v) d")

    ctx = ExitStack()
    with ctx:
        def sb(name, shape, dt=F32):
            return ctx.enter_context(nc.sbuf_tensor(name, shape, dt))

        def bank(name):
            return ctx.enter_context(nc.psum_tensor(name, [P, 512], F32))

        def sem(name):
            return ctx.enter_context(nc.semaphore(name))

        def pair_of_sems(name):
            return [sem(f"{name}{par}") for par in range(PAIR)]

        def chunk(c):
            return slice(c * P, (c + 1) * P)

        cat_sb = sb("cat_sb", [T * CH, P], I32)
        wrap = sb("wrap", [T * CH, P])
        wrapped = sb("wrapped", [T * CH, P])
        clamped = sb("clamped", [T * CH, P])
        base = sb("base", [P, T, CH], I32)
        row_idx = sb("row_idx", [P, T * CH], I32)
        staged = sb("staged", [P, PAIR, CH], I32)

        ident = sb("ident", [P, P])
        w1 = sb("w1", [P, PAIR, H1])
        w1_tail = sb("w1_tail", [P, PAIR, H1])
        w1_num = sb("w1_num", [NUM, H1])
        vec_rows = sb("vec_rows", [KH + 2, P])
        vec_cols = sb("vec_cols", [P, KH + 2])
        b1_col, b2_col, w3_col = vec_cols[:, 0:KH], vec_cols[:, KH:KH + 1], vec_cols[:, KH + 1:KH + 2]
        w_wide_sb = sb("w_wide_sb", [K0, 1])
        w2 = sb("w2", [P, KH, H2])
        b3_sb = sb("b3_sb", [P, 1])
        table_warm = sb("table_warm", [1, 1])

        num_sb = sb("num_sb", [P, CH, K0])
        num_t = sb("num_t", [K0, B])
        wide = sb("wide", [P, CH])
        emb = sb("emb", [P, PAIR, CH, D])
        emb_t = sb("emb_t", [P, PAIR, B])
        emb_tail = sb("emb_tail", [P, CH, PAIR, D])
        emb_tail_t = sb("emb_tail_t", [P, CH, PAIR, P])
        emb_sum = sb("emb_sum", [P, B])
        h1 = sb("h1", [P, KH, B])
        h2 = sb("h2", [H2, B])
        logit = sb("logit", [P, CH])
        y = sb("y", [P, CH, D])

        first_layer = [bank(f"first_layer{k}") for k in range(KH)]
        turn = [bank(f"turn{par}") for par in range(PAIR)]
        mlp = [bank(f"mlp{i}") for i in range(2)]
        scalars = [bank(f"scalars{i}") for i in range(2)]
        idx_bank, num_bank = mlp

        cat_loaded = sem("cat_loaded")
        num_loaded = sem("num_loaded")
        w1_num_loaded = sem("w1_num_loaded")
        small_loaded = sem("small_loaded")
        w1_loaded = pair_of_sems("w1_loaded")
        w1_tail_loaded = sem("w1_tail_loaded")
        ident_steps = sem("ident_steps")
        base_ready = sem("base_ready")
        ones_ready = sem("ones_ready")
        vecs_ready = sem("vecs_ready")
        index_steps = sem("index_steps")
        index_turned = sem("index_turned")
        first_rows_ready = sem("first_rows_ready")
        rows_ready = sem("rows_ready")
        staged_ready = pair_of_sems("staged_ready")
        num_turned = sem("num_turned")
        num_copied = sem("num_copied")
        scalars_done = sem("scalars_done")
        wide_ready = sem("wide_ready")
        slot_free = sem("slot_free")
        gathered = pair_of_sems("gathered")
        turned = pair_of_sems("turned")
        copied = pair_of_sems("copied")
        added = pair_of_sems("added")
        used = pair_of_sems("used")
        tail_gathered = [sem(f"tail_gathered{n}") for n in range(TILES)]
        tail_turned = sem("tail_turned")
        tail_copied = sem("tail_copied")
        tail_added = sem("tail_added")
        h1_low_done = sem("h1_low_done")
        h1_high_done = sem("h1_high_done")
        h1_low_ready = sem("h1_low_ready")
        h1_high_ready = sem("h1_high_ready")
        h2_done = sem("h2_done")
        h2_ready = sem("h2_ready")
        dnn_done = sem("dnn_done")
        logit_ready = sem("logit_ready")
        y_ready = sem("y_ready")
        stored = sem("stored")

        SMALL = 7

        block = ctx.enter_context(nc.Block())

        @block.sync
        def _(sp):
            sp.dma_start(cat_sb[:, :], cat.rearrange("t (c p) -> (t c) p", p=P)).then_inc(cat_loaded, 16)

            def load_w1(step, par, first=False):
                if not first:
                    sp.wait_ge(used[par], step)
                sp.dma_start(w1[:, par, :], W1[bass.ds(NUM + (step * PAIR + par) * D, D), :]
                             ).then_inc(w1_loaded[par], 16)

            for par in range(PAIR):
                load_w1(0, par, first=True)
            sp.dma_start(w1_tail[:, :, :], W1[NUM + TAIL * PAIR * D:NUM + T * D, :].rearrange("(g d) n -> d g n", d=D)
                         ).then_inc(w1_tail_loaded, 16)
            with sp.Fori(1, TAIL) as step:
                for par in range(PAIR):
                    load_w1(step, par)

            for c in range(CH):
                sp.wait_ge(y_ready, c + 1)
                sp.dma_start(out[chunk(c), :], y[:, c, :]).then_inc(stored, 16)
            sp.wait_ge(stored, 16 * CH)

        @block.gpsimd
        def _(gp):
            nc.gpsimd.memset(ident[:, :], 0.0).then_inc(ident_steps, 1)
            gp.wait_ge(ident_steps, 1)
            nc.gpsimd.affine_select(out=ident[:, :], in_=ident[:, :], compare_op=ALU.not_equal, fill=1.0,
                                    base=0, pattern=[[-1, P]], channel_multiplier=1).then_inc(ident_steps, 1)
            nc.gpsimd.iota(base[:, :, :], pattern=[[V, T], [0, CH]], base=0,
                           channel_multiplier=0).then_inc(base_ready, 1)

            def gather(tile, index, landed):
                nc.gpsimd.indirect_dma_start(tile, None, rows, bass.IndirectOffsetOnAxis(ap=index, axis=0)
                                             ).then_inc(landed, 16)

            def column(table, c):
                return row_idx[:, table * CH + c:table * CH + c + 1]

            gp.wait_ge(first_rows_ready, 1)
            for par in range(PAIR):
                for c in range(CH):
                    gather(emb[:, par, c, :], column(par, c), gathered[par])
            with gp.Fori(1, TAIL) as step:
                for par in range(PAIR):
                    gp.wait_ge(staged_ready[par], step)
                    gp.wait_ge(turned[par], step)
                    gp.sem_inc(slot_free, 1)
                    for c in range(CH):
                        gather(emb[:, par, c, :], staged[:, par, c:c + 1], gathered[par])
            gp.wait_ge(rows_ready, 1)
            for c in range(CH):
                for g in range(PAIR):
                    gather(emb_tail[:, c, g, :], column(TAIL * PAIR + g, c), tail_gathered[c * PAIR + g])

        @block.tensor
        def _(pe):
            pe.wait_ge(ident_steps, 2)
            pe.wait_ge(index_steps, 3)
            nc.tensor.transpose(idx_bank[:, 0:T * CH], clamped[:, :],
                                ident[0:T * CH, 0:T * CH]).then_inc(index_turned, 1)
            pe.wait_ge(num_loaded, 16)
            pe.wait_ge(ones_ready, 1)
            for c in range(CH):
                mm = nc.tensor.transpose(num_bank[0:K0, chunk(c)], num_sb[:, c, :], ident[:, :])
            mm.then_inc(num_turned, 1)

            def turn_table(step, par, first=False):
                pe.wait_ge(gathered[par], TABLE_DONE * (step + 1))
                if not first:
                    pe.wait_ge(added[par], step)
                for c in range(CH):
                    mm = nc.tensor.transpose(turn[par][:, chunk(c)], emb[:, par, c, :], ident[:, :])
                mm.then_inc(turned[par], 1)

            def sum_table(step, par):
                pe.wait_ge(w1_loaded[par], 16 * (step + 1))
                pe.wait_ge(copied[par], step + 1)
                for k in range(KH):
                    mm = nc.tensor.matmul(first_layer[k][:, :], w1[:, par, chunk(k)], emb_t[:, par, :],
                                          start=False, stop=False, skip_group_check=True)
                mm.then_inc(used[par], 1)

            pe.wait_ge(num_copied, 1)
            pe.wait_ge(w1_num_loaded, 16)
            for k in range(KH):
                nc.tensor.matmul(first_layer[k][:, :], w1_num[:, chunk(k)], num_t[0:NUM, :], start=True, stop=True)

            def wide_and_vectors():
                pe.wait_ge(small_loaded, 16 * SMALL)
                for c in range(CH):
                    nc.tensor.matmul(scalars[0][:, CH + c:CH + c + 1], num_t[:, chunk(c)], w_wide_sb[:, :],
                                     start=True, stop=True)
                nc.tensor.transpose(scalars[0][:, 2 * CH:2 * CH + KH + 2], vec_rows[:, :],
                                    ident[0:KH + 2, 0:KH + 2]).then_inc(scalars_done, 1)

            turn_table(0, 0, first=True)
            wide_and_vectors()
            turn_table(0, 1, first=True)
            sum_table(0, 0)
            turn_table(1, 0)
            sum_table(0, 1)
            with pe.Fori(1, TAIL - 1) as step:
                turn_table(step, 1)
                sum_table(step, 0)
                turn_table(step + 1, 0)
                sum_table(step, 1)

            def turn_tile(c, g):
                n = c * PAIR + g
                pe.wait_ge(tail_gathered[n], 16)
                if c == 0:
                    pe.wait_ge(added[g], TAIL)
                else:
                    pe.wait_ge(tail_added, n - PAIR + 1)
                nc.tensor.transpose(turn[g][:, 0:P], emb_tail[:, c, g, :], ident[:, :]).then_inc(tail_turned, 1)

            def sum_tile(c, g):
                n = c * PAIR + g
                if n == 0:
                    pe.wait_ge(w1_tail_loaded, 16)
                pe.wait_ge(tail_copied, n + 1)
                for k, (done, ready) in enumerate([(h1_low_done, h1_low_ready), (h1_high_done, h1_high_ready)]):
                    if c >= 1 and g == 0:
                        pe.wait_ge(ready, c)
                    mm = nc.tensor.matmul(first_layer[k][:, chunk(c)], w1_tail[:, g, chunk(k)],
                                          emb_tail_t[:, c, g, :], start=False, stop=False, skip_group_check=True)
                    if g == PAIR - 1:
                        mm.then_inc(done, 1)

            def turn_sum_and_layer2(c):
                pe.wait_ge(tail_added, (c + 1) * PAIR)
                if c >= 2:
                    pe.wait_ge(y_ready, c - 1)
                nc.tensor.transpose(mlp[c % 2][:, P:2 * P], emb_sum[:, chunk(c)], ident[:, :])
                for k, ready in enumerate([h1_low_ready, h1_high_ready]):
                    pe.wait_ge(ready, c + 1)
                    mm = nc.tensor.matmul(mlp[c % 2][:, 0:P], w2[:, k, :], h1[:, k, chunk(c)],
                                          start=(k == 0), stop=(k == KH - 1))
                mm.then_inc(h2_done, 1)

            def layer3(c):
                pe.wait_ge(h2_ready, c + 1)
                if c == 0:
                    pe.wait_ge(vecs_ready, 1)
                if c >= 2:
                    pe.wait_ge(logit_ready, c - 1)
                nc.tensor.matmul(scalars[c % 2][:, c:c + 1], h2[:, chunk(c)], w3_col, start=True, stop=True
                                 ).then_inc(dnn_done, 1)

            sum_table(TAIL - 1, 0)
            turn_table(TAIL - 1, 1)
            turn_tile(0, 0)
            sum_table(TAIL - 1, 1)
            for c in range(CH):
                if c >= 1:
                    turn_tile(c, 0)
                    sum_tile(c - 1, 1)
                turn_tile(c, 1)
                if c >= 2:
                    layer3(c - 2)
                sum_tile(c, 0)
                if c == CH - 1:
                    sum_tile(c, 1)
                if c >= 1:
                    turn_sum_and_layer2(c - 1)
            turn_sum_and_layer2(CH - 1)
            layer3(CH - 2)
            layer3(CH - 1)

        @block.vector
        def _(dve):
            nc.vector.memset(num_sb[:, :, NUM:K0], 1.0).then_inc(ones_ready, 1)
            dve.wait_ge(cat_loaded, 16)
            nc.vector.tensor_scalar(wrap[:, :], cat_sb[:, :], 0.0, float(V), ALU.is_lt, ALU.mult
                                    ).then_inc(index_steps, 1)
            dve.wait_ge(index_steps, 1)
            nc.vector.tensor_tensor(wrapped[:, :], wrap[:, :], cat_sb[:, :], ALU.add).then_inc(index_steps, 1)
            dve.wait_ge(index_steps, 2)
            nc.vector.tensor_scalar(clamped[:, :], wrapped[:, :], 0.0, float(V - 1), ALU.max, ALU.min
                                    ).then_inc(index_steps, 1)
            dve.wait_ge(base_ready, 1)
            dve.wait_ge(index_turned, 1)

            def add_base(lo, hi, ready):
                nc.vector.tensor_tensor(row_idx[:, lo * CH:hi * CH], idx_bank[:, lo * CH:hi * CH],
                                        base[:, lo:hi, :].rearrange("p t c -> p (t c)"), ALU.add).then_inc(ready, 1)

            add_base(0, PAIR, first_rows_ready)
            add_base(PAIR, T, rows_ready)
            dve.wait_ge(rows_ready, 1)

            def stage(step, par, first=False):
                if not first:
                    dve.wait_ge(gathered[par], TABLE_DONE * step)
                nc.vector.tensor_copy(staged[:, par, :], row_idx[:, bass.ds((step * PAIR + par) * CH, CH)]
                                      ).then_inc(staged_ready[par], 1)

            for par in range(PAIR):
                stage(1, par, first=True)

            def add_table(step, par, first=False):
                dve.wait_ge(copied[par], step + 1)
                if first:
                    nc.vector.tensor_copy(emb_sum[:, :], turn[par][:, :]).then_inc(added[par], 1)
                    return
                dve.wait_ge(added[1 - par], step + par)
                nc.vector.tensor_tensor(emb_sum[:, :], turn[par][:, :], emb_sum[:, :], ALU.add
                                        ).then_inc(added[par], 1)

            dve.wait_ge(num_turned, 1)
            nc.vector.tensor_copy(num_t[:, :], num_bank[0:K0, :]).then_inc(num_copied, 1)
            add_table(0, 0, first=True)
            dve.wait_ge(scalars_done, 1)
            dve.wait_ge(small_loaded, 16 * SMALL)
            nc.vector.tensor_scalar(wide[:, :], scalars[0][:, CH:2 * CH], 0.0, b3_sb[:, 0:1], ALU.max, ALU.add
                                    ).then_inc(wide_ready, 1)
            nc.vector.tensor_copy(vec_cols[:, :], scalars[0][:, 2 * CH:2 * CH + KH + 2]).then_inc(vecs_ready, 1)
            add_table(0, 1)
            with dve.Fori(1, TAIL - 1) as step:
                for par in range(PAIR):
                    stage(step + 1, par)
                    add_table(step, par)
            for par in range(PAIR):
                add_table(TAIL - 1, par)

            def add_tile(c, g):
                n = c * PAIR + g
                dve.wait_ge(tail_copied, n + 1)
                if n == 0:
                    dve.wait_ge(added[1], TAIL)
                elif g > 0:
                    dve.wait_ge(tail_added, n)
                nc.vector.tensor_tensor(emb_sum[:, chunk(c)], turn[g][:, 0:P], emb_sum[:, chunk(c)], ALU.add
                                        ).then_inc(tail_added, 1)

            def relu_h1_high(c):
                dve.wait_ge(h1_high_done, c + 1)
                if c == 0:
                    dve.wait_ge(vecs_ready, 1)
                nc.vector.tensor_scalar(h1[:, 1, chunk(c)], first_layer[1][:, chunk(c)], b1_col[:, 1:2], 0.0,
                                        ALU.add, ALU.max).then_inc(h1_high_ready, 1)

            def relu_h2(c):
                dve.wait_ge(h2_done, c + 1)
                nc.vector.tensor_scalar(h2[:, chunk(c)], mlp[c % 2][:, 0:P], b2_col, 0.0, ALU.add, ALU.max
                                        ).then_inc(h2_ready, 1)

            def add_wide(c):
                dve.wait_ge(dnn_done, c + 1)
                if c == 0:
                    dve.wait_ge(wide_ready, 1)
                nc.vector.tensor_tensor(logit[:, c:c + 1], scalars[c % 2][:, c:c + 1], wide[:, c:c + 1], ALU.add
                                        ).then_inc(logit_ready, 1)

            for c in range(CH):
                if c >= 2:
                    relu_h2(c - 2)
                if c >= 1:
                    relu_h1_high(c - 1)
                add_tile(c, 0)
                if c >= 2:
                    add_wide(c - 2)
                add_tile(c, 1)
            relu_h1_high(CH - 1)
            relu_h2(CH - 2)
            relu_h2(CH - 1)
            add_wide(CH - 2)
            add_wide(CH - 1)

        @block.scalar
        def _(act):
            act.wait_ge(ones_ready, 1)
            act.dma_start(num_sb[:, :, 0:NUM], num.rearrange("(c p) k -> p c k", p=P)).then_inc(num_loaded, 16)
            act.dma_start(w1_num[:, :], W1[0:NUM, :]).then_inc(w1_num_loaded, 16)
            act.dma_start(w_wide_sb[0:NUM, :], w_wide).then_inc(small_loaded, 16)
            act.dma_start(w_wide_sb[NUM:K0, :], b_wide.unsqueeze(0)).then_inc(small_loaded, 16)
            act.dma_start(b3_sb[:, :], b3.partition_broadcast(P)).then_inc(small_loaded, 16)
            act.dma_start(vec_rows[0:KH, :], b1.rearrange("(k p) -> k p", p=P)).then_inc(small_loaded, 16)
            act.dma_start(vec_rows[KH:KH + 1, :], b2.unsqueeze(0)).then_inc(small_loaded, 16)
            act.dma_start(vec_rows[KH + 1:KH + 2, :], W3.rearrange("p a -> a p")).then_inc(small_loaded, 16)
            act.dma_start(w2[:, :, :], W2.rearrange("(k p) n -> p k n", p=P)).then_inc(small_loaded, 16)
            act.wait_ge(ident_steps, 2)
            nc.scalar.activation(table_warm[:, :], ident[0:1, 0:1], ACT.Sigmoid)

            def copy_table(step, par, first=False):
                act.wait_ge(turned[par], step + 1)
                if not first:
                    act.wait_ge(used[par], step)
                nc.scalar.copy(emb_t[:, par, :], turn[par][:, :]).then_inc(copied[par], 1)

            for par in range(PAIR):
                copy_table(0, par, first=True)
            with act.Fori(1, TAIL) as step:
                for par in range(PAIR):
                    copy_table(step, par)

            def copy_tile(c, g):
                act.wait_ge(tail_turned, c * PAIR + g + 1)
                nc.scalar.copy(emb_tail_t[:, c, g, :], turn[g][:, 0:P]).then_inc(tail_copied, 1)

            def relu_h1_low(c):
                act.wait_ge(h1_low_done, c + 1)
                if c == 0:
                    act.wait_ge(vecs_ready, 1)
                nc.scalar.activation(h1[:, 0, chunk(c)], first_layer[0][:, chunk(c)], ACT.Relu,
                                     bias=b1_col[:, 0:1]).then_inc(h1_low_ready, 1)

            def squash(c):
                act.wait_ge(logit_ready, c + 1)
                nc.scalar.activation(y[:, c, :], mlp[c % 2][:, P:2 * P], ACT.Sigmoid,
                                     bias=logit[:, c:c + 1]).then_inc(y_ready, 1)

            for c in range(CH):
                copy_tile(c, 0)
                if c >= 1:
                    relu_h1_low(c - 1)
                copy_tile(c, 1)
                if c >= 2:
                    squash(c - 2)
            relu_h1_low(CH - 1)
            squash(CH - 2)
            squash(CH - 1)


_NAMES = ["r_numerical", "r_cat_features", "L0_rec_tables", "L0_rec_w_wide", "L0_rec_b_wide", "L0_rec_W1",
          "L0_rec_b1", "L0_rec_W2", "L0_rec_b2", "L0_rec_W3", "L0_rec_b3"]


def kernel(**inputs):
    import numpy as np
    import concourse.bacc as bacc
    from concourse import mybir
    from concourse.bass_utils import run_bass_kernel_spmd

    nc = bacc.Bacc("TRN2", target_bir_lowering=False, num_devices=1)
    arrays, args = {}, []
    for name in _NAMES:
        a = np.ascontiguousarray(inputs[name])
        arrays[f"in_{name}"] = a
        args.append(nc.dram_tensor(f"in_{name}", a.shape, mybir.dt.from_np(a.dtype), kind="ExternalInput").ap())
    shape = (inputs["r_numerical"].shape[0], inputs["L0_rec_tables"].shape[2])
    args.append(nc.dram_tensor("out", shape, mybir.dt.float32, kind="ExternalOutput").ap())
    build(nc, *args)
    result = run_bass_kernel_spmd(nc, [arrays], core_ids=[0])
    return result.results[0]["out"]
```
